# Optimizing a Trainium2 kernel written in Bass

```python
import numpy as np
import jax
import jax.numpy as jnp

def _softmax(x, axis=-1):
    return jax.nn.softmax(x, axis=axis)

def _gelu(x):
    return jax.nn.gelu(x, approximate=True)

def _silu(x):
    return jax.nn.silu(x)

def _sigmoid(x):
    return jax.nn.sigmoid(x)

def _layernorm(x, axis=-1, eps=1e-05):
    m = jnp.mean(x, axis=axis, keepdims=True)
    v = jnp.var(x, axis=axis, keepdims=True)
    return (x - m) / jnp.sqrt(v + eps)

def _scatter_add(tgt, idx, src, axis=0):
    return tgt.at[idx].add(src)

def _segment_sum(src, seg, n):
    return jax.ops.segment_sum(src, seg, n)
kernel_name = 'mk_conv_preact_d1_conv_nchw256_r4_00f009'

def setup_inputs(seed: int=0):
    np.random.seed(seed)
    _w = jnp.asarray

    def _rec_inputs():
        import jax
        import jax.numpy as jnp
        _gk = jax.random.key(seed)
        x = -0.0002091 + 1 * jax.random.normal(jax.random.fold_in(_gk, 1), (32, 64, 56, 56), jnp.float32)
        return x
    x = _rec_inputs()

    def _L0_conv_setup():
        import jax, jax.numpy as jnp
        import numpy as np
        BOUND = 1.0
        key = jax.random.key(seed)
        kx, kw = jax.random.split(key)
        x = jax.random.normal(kx, (32, 64, 56, 56), dtype=jnp.float32)
        fan_in = 64 * 3 * 3
        fan_out = 64 * 3 * 3
        std = 2.0 * np.sqrt(2.0 / (fan_in + fan_out))
        W = jax.random.normal(kw, (64, 64, 3, 3), dtype=jnp.float32) * std
        return {'x': x, 'W': W}
    _L0_conv_all = _L0_conv_setup()
    _L0_conv_in = {k: v for k, v in _L0_conv_all.items() if k in ('W',)}
    del _L0_conv_all
    return {'x': x, 'L0_conv_W': _L0_conv_in['W']}

def reference(x, L0_conv_W):
    import jax
    import jax.numpy as jnp

    def _L0_conv_ref(x, W):
        import jax, jax.numpy as jnp
        import numpy as np
        BOUND = 1.0
        cw = jnp.clip(W, -BOUND, BOUND)
        bw = cw + jax.lax.stop_gradient(jnp.sign(W) - cw)
        out = jax.lax.conv_general_dilated(x, bw, window_strides=(1, 1), padding=((1, 1), (1, 1)), dimension_numbers=('NCHW', 'OIHW', 'NCHW'))
        return out

    def _gn(v, G=32, eps=1e-05):
        B_, C_, H_, W_ = v.shape
        g = v.reshape(B_, G, C_ // G, H_, W_)
        m = jnp.mean(g, axis=(2, 3, 4), keepdims=True)
        s = jnp.var(g, axis=(2, 3, 4), keepdims=True)
        return ((g - m) / jnp.sqrt(s + eps)).reshape(v.shape)

    def _ln_c(v, eps=1e-06):
        m = jnp.mean(v, axis=1, keepdims=True)
        s = jnp.var(v, axis=1, keepdims=True)
        return (v - m) / jnp.sqrt(s + eps)

    def _ln_t(v, eps=1e-05):
        m = jnp.mean(v, axis=-1, keepdims=True)
        s = jnp.var(v, axis=-1, keepdims=True)
        return (v - m) / jnp.sqrt(s + eps)

    def _to_tokens(v):
        B_, C_, H_, W_ = v.shape
        return v.reshape(B_, C_, H_ * W_).transpose(0, 2, 1)

    def _from_tokens(t, like):
        B_, C_, H_, W_ = like.shape
        return t.transpose(0, 2, 1).reshape(B_, C_, H_, W_)
    x = x + _L0_conv_ref(_gn(x), L0_conv_W)
    return x

_drawn_inputs = setup_inputs


def setup_inputs(seed=0):
    import zlib

    import numpy as np

    out = dict(_drawn_inputs(seed))
    spreads = {}
    factors = {}
    for name, (base, spread) in spreads.items():
        noise = np.random.default_rng([zlib.crc32(name.encode()), seed]).standard_normal(out[name].shape)
        drawn = base * np.exp(spread * noise) if base else spread * noise
        out[name] = jnp.asarray(drawn.astype(out[name].dtype))
    for name, factor in factors.items():
        out[name] = (out[name] * factor).astype(out[name].dtype)
    return out
```

```python
from contextlib import ExitStack

import concourse.bass as bass
from concourse import mybir


F32 = mybir.dt.float32
F16 = mybir.dt.float16
ALU = mybir.AluOpType
ACT = mybir.ActivationFunctionType

GROUPS = 32
EPS = 1e-5
SCALE = 2.0 ** 9

XRING = 4
TRING = 2
NRING = 2


def conv_preact_kernel(nc: bass.Bass, x: bass.AP, w: bass.AP, out: bass.AP):
    B, C, H, W = x.shape
    CO, _, KH, KW = w.shape
    assert 2 * C == 128 and CO == C and C // GROUPS == 2 and KH == KW == 3
    assert (C // GROUPS) * H * W * SCALE ** 2 < 65504.0 ** 2
    PAIRS = B // 2
    HW = H * W
    PW = W + 2
    PHW = (H + 2) * PW
    BR = 8
    BN = BR * W
    NB = H // BR
    TAPS = KH * KW
    GR = [range(0, 2), range(2, 4), range(4, 6), range(6, 7)]
    NG = len(GR)
    assert BN <= 512 and H % BR == 0 and GR[-1][-1] == NB - 1
    assert PAIRS % XRING == 0 and PAIRS > XRING and XRING % TRING == 0 and TRING == NRING

    FIRST = [(0, 14), (14, 28), (28, 42), (42, 56)]
    REST = [(0, 28), (28, 56)]
    NF, NR = len(FIRST), len(REST)
    PIECE = 14

    def chunks(first):
        return FIRST if first else REST

    def chunks_done(pair, c):
        return (pair - 1) * NR + NF + c + 1

    def chunk_of_row(row, first):
        return next(c for c, (a, b) in enumerate(chunks(first)) if a <= row < b)

    x_pairs = x.rearrange("(n b) c h w -> n (b c) (h w)", b=2)
    out_pairs = out.rearrange("(n b) c h w -> n (b c) (h w)", b=2)

    with ExitStack() as ctx:
        def sb(name, shape, dt):
            return ctx.enter_context(nc.sbuf_tensor(name, shape, dt))

        def sem(name):
            return ctx.enter_context(nc.semaphore(name))

        xbuf = sb("xbuf", [128, XRING, HW], F32)
        xnorm = sb("xnorm", [128, NRING, HW], F32)
        halves = sb("halves", [128, TRING, 2, PHW], F16)
        w_raw = sb("w_raw", [CO, C * TAPS], F32)
        w_pos = sb("w_pos", [CO, C * TAPS], F32)
        w_sign = sb("w_sign", [CO, TAPS, 2, C], F16)
        w_taps = sb("w_taps", [128, TAPS, CO], F16)
        ident = sb("ident", [CO, CO], F16)
        stats = sb("stats", [128, NB, 6], F32)
        own = sb("own", [128, 2], F32)
        other = sb("other", [128, 2], F32)
        small = sb("small", [128, 8], F32)
        coef = sb("coef", [128, XRING, 2], F32)
        zero = sb("zero", [128, 1], F32)
        psum = ctx.enter_context(nc.psum_tensor("psum", [128, 8, 512], F32))

        x0_loaded = [sem(f"x0_loaded{g}") for g in range(NG)]
        loaded = [sem(f"loaded{s}") for s in range(XRING)]
        stored = [sem(f"stored{s}") for s in range(XRING)]
        w_loaded = sem("w_loaded")
        w_step = sem("w_step")
        ident_step = sem("ident_step")
        zero_ready = sem("zero_ready")
        borders_ready = sem("borders_ready")
        w_turned = sem("w_turned")
        w_ready = sem("w_ready")
        stat_step = sem("stat_step")
        var_ready = sem("var_ready")
        std_ready = sem("std_ready")
        coef_ready = sem("coef_ready")
        xnorm_ready = sem("xnorm_ready")
        hi_ready = sem("hi_ready")
        hi_a_ready = sem("hi_a_ready")
        lo_a_ready = sem("lo_a_ready")
        lo_b_ready = sem("lo_b_ready")
        conv_done = sem("conv_done")
        evacuated = sem("evacuated")

        def rows(t, a, b):
            return t[:, a * W:b * W].rearrange("p (h w) -> p h w", w=W)

        def inner(img, slot, lanes, a, b):
            v = halves[lanes, slot, img, :].rearrange("p (h w) -> p h w", w=PW)
            return v[:, 1 + a:1 + b, 1:1 + W]

        LOW, HIGH, ALL = slice(0, 64), slice(64, 128), slice(0, 128)

        def loads_done(it, s):
            return 16 * (it + 1) if s else 16 * it

        block = ctx.enter_context(nc.Block())

        @block.sync
        def _(sp):
            for g, blocks in enumerate(GR):
                part = slice(blocks[0] * BN, (blocks[-1] + 1) * BN)
                sp.dma_start(xbuf[:, 0, part], x_pairs[0][:, part]).then_inc(x0_loaded[g], 16)
            for s in range(1, XRING):
                sp.dma_start(xbuf[:, s, :], x_pairs[s]).then_inc(loaded[s], 16)

            def store(it, s, parts):
                for groups in parts:
                    sp.wait_ge(evacuated, (it * XRING + s) * NG + groups[-1] + 1)
                    part = slice(GR[groups[0]][0] * BN, (GR[groups[-1]][-1] + 1) * BN)
                    sp.dma_start(out_pairs[it * XRING + s][:, part],
                                 xbuf[:, s, part]).then_inc(stored[s], 16)

            with sp.Fori(0, PAIRS // XRING - 1) as it:
                for s in range(XRING):
                    store(it, s, [range(0, 2), range(2, NG)])
                    sp.wait_ge(stored[s], (it + 1) * 32)
                    sp.dma_start(xbuf[:, s, :], x_pairs[(it + 1) * XRING + s]).then_inc(loaded[s], 16)
            last = PAIRS // XRING - 1
            for s in range(XRING):
                store(last, s, [range(g, g + 1) for g in range(NG)] if s == XRING - 1
                      else [range(0, 2), range(2, NG)])
            for s in range(XRING):
                n = NG if s == XRING - 1 else 2
                sp.wait_ge(stored[s], last * 32 + n * 16)

        @block.gpsimd
        def _(pool):
            nc.gpsimd.memset(ident[:], 0.0).then_inc(ident_step, 1)
            pool.wait_ge(ident_step, 1)
            nc.gpsimd.affine_select(out=ident[:], in_=ident[:], compare_op=ALU.not_equal, fill=1.0,
                                    base=0, pattern=[[-1, CO]], channel_multiplier=1).then_inc(ident_step, 1)
            tiles = halves[:].rearrange("p t i n -> p (t i) n")
            nc.gpsimd.memset(tiles[:, :, 0:PW - 1], 0.0).then_inc(borders_ready, 1)
            nc.gpsimd.memset(tiles[:, :, PHW - PW + 1:PHW], 0.0).then_inc(borders_ready, 1)
            sides = tiles[:, :, PW - 1:PHW - 1].rearrange("p t (h w) -> p t h w", w=PW)[:, :, :, 0:2]
            nc.gpsimd.memset(sides, 0.0).then_inc(borders_ready, 1)

            def lo_a(pair, slot, first):
                for c, (a, b) in enumerate(chunks(first)):
                    pool.wait_ge(hi_ready, c + 1 if first else chunks_done(pair, c))
                    for r in range(a, b, PIECE):
                        nc.gpsimd.tensor_tensor(inner(0, slot, LOW, r, r + PIECE),
                                                rows(xnorm[LOW, slot, :], r, r + PIECE),
                                                inner(1, slot, LOW, r, r + PIECE),
                                                ALU.subtract).then_inc(lo_a_ready, 1)

            lo_a(0, 0, True)
            lo_a(1, 1, False)
            with pool.Fori(1, PAIRS // TRING) as it:
                for s in range(TRING):
                    lo_a(it * TRING + s, s, False)

        PIECES = H // PIECE

        def pieces_done(pair, row):
            return pair * PIECES + -(-row // PIECE)

        @block.scalar
        def _(act):
            act.dma_start(w_raw[:], w.rearrange("o c h w -> o (c h w)")).then_inc(w_loaded, 16)

            def deviation(pair, s):
                act.wait_ge(var_ready, pair + 1)
                nc.scalar.activation(small[:, 4:5], small[:, 3:4], ACT.Sqrt,
                                     bias=zero[:]).then_inc(std_ready, 1)

            def normalise(pair, s, slot, a, b):
                nc.scalar.activation(xnorm[:, slot, a * W:b * W], xbuf[:, s, a * W:b * W], ACT.Identity,
                                     bias=coef[:, s, 1:2], scale=coef[:, s, 0:1]).then_inc(xnorm_ready, 1)

            def hi(slot, a, b):
                nc.scalar.copy(inner(1, slot, ALL, a, b),
                               rows(xnorm[:, slot, :], a, b)).then_inc(hi_ready, 1)

            def hi_a(slot, a, b):
                nc.scalar.copy(inner(0, slot, HIGH, a, b),
                               rows(xnorm[LOW, slot, :], a, b)).then_inc(hi_a_ready, 1)

            act.wait_ge(zero_ready, 1)
            deviation(0, 0)
            act.wait_ge(w_turned, 1)
            nc.scalar.copy(w_taps[:, 0:8, :], psum[:, 0, :].rearrange("p (t o) -> p t o", o=CO)).then_inc(w_ready, 1)
            nc.scalar.copy(w_taps[:, 8, :], psum[:, 1, 0:CO]).then_inc(w_ready, 1)
            act.wait_ge(coef_ready, 2)
            for c, (a, b) in enumerate(FIRST):
                normalise(0, 0, 0, a, b)
                act.wait_ge(xnorm_ready, c + 1)
                hi(0, a, b)
                hi_a(0, a, b)

            def pair_after(pair, s, slot, free):
                deviation(pair, s)
                act.wait_ge(coef_ready, 2 * (pair + 1))
                if free:
                    act.wait_ge(lo_b_ready, chunks_done(pair - NRING, NR - 1))
                for a, b in REST:
                    normalise(pair, s, slot, a, b)
                if free:
                    act.wait_ge(conv_done, (pair - TRING + 1) * NB)
                for c, (a, b) in enumerate(REST):
                    act.wait_ge(xnorm_ready, chunks_done(pair, c))
                    hi(slot, a, b)
                    hi_a(slot, a, b)

            pair_after(1, 1, 1, False)
            act.wait_ge(lo_b_ready, NF)
            pair_after(2, 2, 0, True)
            pair_after(3, 3, 1, True)
            with act.Fori(1, PAIRS // XRING) as it:
                for s in range(XRING):
                    pair_after(it * XRING + s, s, s % TRING, True)

        @block.vector
        def _(dve):
            STEPS = 10

            nc.vector.memset(zero[:], 0.0).then_inc(zero_ready, 1)

            dve.wait_ge(w_loaded, 16)
            nc.vector.tensor_scalar(w_pos[:], w_raw[:], 0.0, -1.0, ALU.is_gt, ALU.add).then_inc(w_step, 1)
            dve.wait_ge(w_step, 1)
            for j in range(2):
                nc.vector.scalar_tensor_tensor(w_sign[:, :, j, :],
                                               w_raw[:].rearrange("o (c t) -> o t c", t=TAPS), 0.0,
                                               w_pos[:].rearrange("o (c t) -> o t c", t=TAPS),
                                               ALU.is_ge, ALU.add).then_inc(w_step, 1)

            def block_stats(s, blocks):
                for n in blocks:
                    nc.vector.bn_stats(stats[:, n, :], xbuf[:, s, n * BN:(n + 1) * BN]).then_inc(stat_step, 1)

            def blocks_done(pair):
                dve.wait_ge(stat_step, pair * (NB + STEPS) + NB)

            def variance(pair):
                n = pair * (NB + STEPS) + NB
                nc.vector.bn_aggr(own[:], stats[:]).then_inc(stat_step, 1)
                dve.wait_ge(stat_step, n + 1)
                nc.vector.tensor_scalar(small[:, 7:8], own[:, 0:1], -0.5, None, ALU.mult).then_inc(stat_step, 1)
                nc.vector.stream_shuffle(other[:], own[:], [i ^ 1 for i in range(32)]).then_inc(stat_step, 1)
                dve.wait_ge(stat_step, n + 3)
                nc.vector.tensor_scalar(small[:, 0:1], own[:, 0:1], other[:, 0:1], 0.5 / SCALE,
                                        ALU.subtract, ALU.mult).then_inc(stat_step, 1)
                nc.vector.tensor_scalar(small[:, 1:2], own[:, 1:2], other[:, 1:2], 0.5 / SCALE ** 2,
                                        ALU.add, ALU.mult).then_inc(stat_step, 1)
                nc.vector.tensor_scalar(small[:, 6:7], other[:, 0:1], -0.5, small[:, 7:8],
                                        ALU.mult, ALU.add).then_inc(stat_step, 1)
                dve.wait_ge(stat_step, n + 6)
                nc.vector.tensor_scalar(small[:, 2:3], small[:, 0:1], small[:, 0:1], EPS / SCALE ** 2,
                                        ALU.mult, ALU.add).then_inc(stat_step, 1)
                dve.wait_ge(stat_step, n + 7)
                nc.vector.tensor_tensor(small[:, 3:4], small[:, 1:2], small[:, 2:3],
                                        ALU.add).then_inc(var_ready, 1)

            def coefficients(pair, s):
                n = pair * (NB + STEPS) + NB + 7
                dve.wait_ge(std_ready, pair + 1)
                nc.vector.reciprocal(small[:, 5:6], small[:, 4:5]).then_inc(stat_step, 1)
                dve.wait_ge(stat_step, n + 1)
                dve.wait_ge(var_ready, pair + 1)
                nc.vector.tensor_scalar(small[:, 0:1], small[:, 3:4], small[:, 5:6], small[:, 5:6],
                                        ALU.mult, ALU.mult).then_inc(stat_step, 1)
                dve.wait_ge(stat_step, n + 2)
                nc.vector.tensor_scalar(small[:, 1:2], small[:, 0:1], -0.5, 1.5,
                                        ALU.mult, ALU.add).then_inc(stat_step, 1)
                dve.wait_ge(stat_step, n + 3)
                nc.vector.tensor_scalar(coef[:, s, 0:1], small[:, 1:2], small[:, 5:6], None,
                                        ALU.mult).then_inc(coef_ready, 1)
                nc.vector.tensor_scalar(coef[:, s, 1:2], small[:, 1:2], small[:, 5:6], small[:, 6:7],
                                        ALU.mult, ALU.mult).then_inc(coef_ready, 1)

            def lo_b(pair, slot, c, first=False):
                a, b = chunks(first)[c]
                dve.wait_ge(hi_ready, c + 1 if first else chunks_done(pair, c))
                dve.wait_ge(lo_a_ready, pieces_done(pair, b))
                nc.vector.tensor_tensor(inner(1, slot, LOW, a, b), rows(xnorm[HIGH, slot, :], a, b),
                                        inner(1, slot, HIGH, a, b), ALU.subtract).then_inc(lo_b_ready, 1)

            def evacuate(pair, s, g):
                b0, n = GR[g][0], len(GR[g])
                dve.wait_ge(conv_done, pair * NB + b0 + n)
                x_part = xbuf[:, s, b0 * BN:(b0 + n) * BN].rearrange("p (n m) -> p n m", m=BN)
                nc.vector.scalar_tensor_tensor(x_part, psum[:, b0:b0 + n, 0:BN], 1.0 / SCALE, x_part,
                                               ALU.mult, ALU.add).then_inc(evacuated, 1)

            for g, blocks in enumerate(GR):
                dve.wait_ge(x0_loaded[g], 16)
                block_stats(0, blocks)
            blocks_done(0)
            variance(0)
            coefficients(0, 0)
            dve.wait_ge(loaded[1], loads_done(0, 1))
            for c in range(NF):
                block_stats(1, GR[c])
                lo_b(0, 0, c, True)
            blocks_done(1)
            variance(1)
            coefficients(1, 1)

            def pair_step(it, s, more, most):
                pair = it * XRING + s
                if most:
                    turn, slot = it + (s + 2) // XRING, (s + 2) % XRING
                    dve.wait_ge(loaded[slot], loads_done(turn, slot))
                    block_stats(slot, range(NB))
                    blocks_done(pair + 2)
                evacuate(pair, s, 0)
                if most:
                    variance(pair + 2)
                if more:
                    lo_b(pair + 1, (s + 1) % TRING, 0)
                evacuate(pair, s, 1)
                if most:
                    coefficients(pair + 2, slot)
                evacuate(pair, s, 2)
                if more:
                    lo_b(pair + 1, (s + 1) % TRING, 1)
                evacuate(pair, s, 3)

            with dve.Fori(0, PAIRS // XRING - 1) as it:
                for s in range(XRING):
                    pair_step(it, s, True, True)
            for s in range(XRING):
                pair_step(PAIRS // XRING - 1, s, s + 1 < XRING, s + 2 < XRING)

        @block.tensor
        def _(pe):
            pe.wait_ge(ident_step, 2)
            pe.wait_ge(w_step, 3)
            for t in range(TAPS):
                mm = pe.matmul(psum[:, t // 8, (t % 8) * CO:(t % 8 + 1) * CO],
                               w_sign[:, t, :, :].rearrange("o j c -> o (j c)"), ident[:],
                               start=True, stop=True)
            mm.then_inc(w_turned, 1)

            def convolve(pair, slot, first=False, banks_used=True):
                for n in range(NB):
                    last_row = min((n + 1) * BR, H - 1)
                    c = chunk_of_row(last_row, first)
                    if n == 0 or c != chunk_of_row(min(n * BR, H - 1), first):
                        done = c + 1 if first else chunks_done(pair, c)
                        pe.wait_ge(hi_a_ready, done)
                        pe.wait_ge(lo_a_ready, pieces_done(pair, chunks(first)[c][1]))
                        pe.wait_ge(lo_b_ready, done)
                    if banks_used and n in [g[0] for g in GR]:
                        g = [g[0] for g in GR].index(n)
                        pe.wait_ge(evacuated, (pair - 1) * NG + g + 1)
                    for t in range(TAPS):
                        dy, dx = t // KW, t % KW
                        for img, cols in enumerate((LOW, HIGH)):
                            v = halves[:, slot, img, :].rearrange("p (h w) -> p h w", w=PW)
                            mm = pe.matmul(psum[cols, n, 0:BN], w_taps[:, t, :],
                                           v[:, n * BR + dy:n * BR + dy + BR, dx:dx + W],
                                           start=(t == 0), stop=(t == TAPS - 1))
                    mm.then_inc(conv_done, 1)

            pe.wait_ge(w_ready, 2)
            pe.wait_ge(borders_ready, 3)
            convolve(0, 0, first=True, banks_used=False)
            convolve(1, 1)
            with pe.Fori(1, PAIRS // TRING) as it:
                for s in range(TRING):
                    convolve(it * TRING + s, s)


_INS = ["x", "L0_conv_W"]


def kernel(**inputs):
    import numpy as _np
    import concourse.bacc as _bacc
    from concourse import mybir as _mybir
    from concourse.bass_utils import run_bass_kernel_spmd as _run

    nc = _bacc.Bacc("TRN2", target_bir_lowering=False, num_devices=1)
    arrays, args = {}, []
    for name in _INS:
        a = _np.ascontiguousarray(inputs[name])
        arrays[f"in_{name}_dram"] = a
        args.append(nc.dram_tensor(f"in_{name}_dram", a.shape, _mybir.dt.from_np(a.dtype), kind="ExternalInput").ap())
    shape = tuple(inputs["x"].shape)
    args.append(nc.dram_tensor("out_0_dram", shape, _mybir.dt.float32, kind="ExternalOutput").ap())
    conv_preact_kernel(nc, *args)
    r = _run(nc, [arrays], core_ids=[0])
    return r.results[0]["out_0_dram"]
```

```python
from contextlib import ExitStack

import concourse.bass as bass
from concourse import mybir


F32 = mybir.dt.float32
F16 = mybir.dt.float16
ALU = mybir.AluOpType
ACT = mybir.ActivationFunctionType

GROUPS = 32
EPS = 1e-5
SCALE = 2.0 ** 9

XRING = 4
ORING = 2
TRING = 2
NRING = 2
WARM_UP = 10


def conv_preact_kernel(nc: bass.Bass, x: bass.AP, w: bass.AP, out: bass.AP):
    B, C, H, W = x.shape
    CO, _, KH, KW = w.shape
    assert 2 * C == 128 and CO == C and C // GROUPS == 2 and KH == KW == 3
    assert (C // GROUPS) * H * W * SCALE ** 2 < 65504.0 ** 2
    PAIRS = B // 2
    HW = H * W
    LEAD = 2
    PW = LEAD + W
    PHW = (H + 1) * PW
    BR = 8
    BN = BR * W
    NB = H // BR
    TAPS = KH * KW
    GR = [range(0, 2), range(2, 4), range(4, 6), range(6, 7)]
    NG = len(GR)
    PARTS = [range(0, 2), range(2, NG)]
    NP = len(PARTS)

    def part_of(groups):
        return slice(GR[groups[0]][0] * BN, (GR[groups[-1]][-1] + 1) * BN)
    assert BN <= 512 and H % BR == 0 and GR[-1][-1] == NB - 1
    assert PAIRS % XRING == 0 and PAIRS > XRING and XRING % TRING == 0 and TRING == NRING

    FIRST = [(0, 9), (9, 25), (25, 41), (41, 56)]
    REST = [(0, 28), (28, 56)]
    NF, NR = len(FIRST), len(REST)
    PIECE = 14

    def chunks(first):
        return FIRST if first else REST

    def chunks_done(pair, c):
        return (pair - 1) * NR + NF + c + 1

    def chunk_of_row(row, first):
        return next(c for c, (a, b) in enumerate(chunks(first)) if a <= row < b)

    x_pairs = x.rearrange("(n b) c h w -> n (b c) (h w)", b=2)
    out_pairs = out.rearrange("(n b) c h w -> n (b c) (h w)", b=2)

    with ExitStack() as ctx:
        def sb(name, shape, dt):
            return ctx.enter_context(nc.sbuf_tensor(name, shape, dt))

        def sem(name):
            return ctx.enter_context(nc.semaphore(name))

        xbuf = sb("xbuf", [128, XRING, HW], F32)
        obuf = sb("obuf", [128, ORING, HW], F32)
        xnorm = sb("xnorm", [128, NRING, HW], F32)
        halves = sb("halves", [128, TRING, 2, PHW], F16)
        w_raw = sb("w_raw", [CO, C * TAPS], F32)
        w_pos = sb("w_pos", [CO, C * TAPS], F32)
        w_sign = sb("w_sign", [CO, TAPS, C], F16)
        w_taps = sb("w_taps", [128, TAPS, CO], F16)
        ident = sb("ident", [CO, CO], F16)
        stats = sb("stats", [128, 2, NB, 6], F32)
        own = sb("own", [128, 2], F32)
        other = sb("other", [128, 2], F32)
        half_mean, neg_mean, apart, within, square, var, std, inv, ratio, factor = [
            sb(name, [128, 1], F32) for name in
            ("half_mean", "neg_mean", "apart", "within", "square", "var", "std", "inv", "ratio", "factor")]
        coef = sb("coef", [128, XRING, 2], F32)
        zero = sb("zero", [128, 1], F32)
        warm = sb("warm", [128, 1], F32)
        psum = ctx.enter_context(nc.psum_tensor("psum", [128, 8, 512], F32))

        x0_loaded = [sem(f"x0_loaded{g}") for g in range(NG)]
        loaded = [[sem(f"loaded{s}_{h}") for h in range(NP)] for s in range(XRING)]
        stored = [[sem(f"stored{s}_{h}") for h in range(NP)] for s in range(ORING)]
        last_stored = sem("last_stored")
        w_loaded = sem("w_loaded")
        w_step = sem("w_step")
        ident_step = sem("ident_step")
        zero_ready = sem("zero_ready")
        borders_ready = sem("borders_ready")
        w_turned = sem("w_turned")
        w_ready = sem("w_ready")
        blocks_ready = sem("blocks_ready")
        coef_step = sem("coef_step")
        var_ready = sem("var_ready")
        std_ready = sem("std_ready")
        coef_ready = sem("coef_ready")
        xnorm_ready = sem("xnorm_ready")
        hi_ready = sem("hi_ready")
        hi_a_ready = sem("hi_a_ready")
        lo_a_ready = sem("lo_a_ready")
        lo_b_ready = sem("lo_b_ready")
        conv_done = sem("conv_done")
        evacuated = sem("evacuated")

        def rows(t, a, b):
            return t[:, a * W:b * W].rearrange("p (h w) -> p h w", w=W)

        def inner(img, slot, lanes, a, b):
            v = halves[lanes, slot, img, :].rearrange("p (h w) -> p h w", w=PW)
            return v[:, a:b, LEAD:LEAD + W]

        LOW, HIGH, ALL = slice(0, 64), slice(64, 128), slice(0, 128)

        def loads_done(it, s):
            return 16 * (it + 1) if s else 16 * it

        def stores_done(it, s):
            return it * (XRING // ORING) + s // ORING + 1

        block = ctx.enter_context(nc.Block())

        @block.sync
        def _(sp):
            for g in range(NG):
                part = part_of([g])
                sp.dma_start(xbuf[:, 0, part], x_pairs[0][:, part]).then_inc(x0_loaded[g], 16)
            for s in range(1, XRING):
                for h, groups in enumerate(PARTS):
                    part = part_of(groups)
                    sp.dma_start(xbuf[:, s, part], x_pairs[s][:, part]).then_inc(loaded[s][h], 16)

            def store(pair, s, groups, done):
                sp.wait_ge(evacuated, pair * NG + groups[-1] + 1)
                part = part_of(groups)
                sp.dma_start(out_pairs[pair][:, part], obuf[:, s % ORING, part]).then_inc(done, 16)

            def store_and_load(pair, it, s, first=False):
                for h, groups in enumerate(PARTS):
                    part = part_of(groups)
                    sp.wait_ge(evacuated, pair * NG + groups[-1] + 1)
                    if not first:
                        before = (s - 1) % ORING
                        sp.wait_ge(stored[before][h], 16 * stores_done(it, s - 1))
                    sp.dma_start(xbuf[:, s, part], x_pairs[pair + XRING][:, part]).then_inc(loaded[s][h], 16)
                    store(pair, s, groups, stored[s % ORING][h])

            for s in range(XRING):
                store_and_load(s, 0, s, first=(s == 0))
            with sp.Fori(1, PAIRS // XRING - 1) as it:
                for s in range(XRING):
                    store_and_load(it * XRING + s, it, s)
            for s in range(XRING):
                pair = PAIRS - XRING + s
                if s < XRING - 1:
                    for h, groups in enumerate(PARTS):
                        store(pair, s, groups, stored[s % ORING][h])
                else:
                    for g in range(NG):
                        store(pair, s, [g], last_stored)
            sp.wait_ge(last_stored, 16 * NG)
            for s in range(XRING - ORING - 1, XRING - 1):
                for h in range(NP):
                    sp.wait_ge(stored[s % ORING][h], 16 * stores_done(PAIRS // XRING - 1, s))

        @block.gpsimd
        def _(pool):
            nc.gpsimd.memset(ident[:], 0.0).then_inc(ident_step, 1)
            pool.wait_ge(ident_step, 1)
            nc.gpsimd.affine_select(out=ident[:], in_=ident[:], compare_op=ALU.not_equal, fill=1.0,
                                    base=0, pattern=[[-1, CO]], channel_multiplier=1).then_inc(ident_step, 1)
            fronts = halves[:].rearrange("p t i (h w) -> p (t i) h w", w=PW)[:, :, :, 0:LEAD]
            nc.gpsimd.memset(fronts, 0.0).then_inc(borders_ready, 1)

            def lo_a(pair, slot, first):
                for c, (a, b) in enumerate(chunks(first)):
                    pool.wait_ge(hi_ready, c + 1 if first else chunks_done(pair, c))
                    piece = b - a if first else PIECE
                    for r in range(a, b, piece):
                        nc.gpsimd.tensor_tensor(inner(0, slot, LOW, r, r + piece),
                                                rows(xnorm[LOW, slot, :], r, r + piece),
                                                inner(1, slot, LOW, r, r + piece),
                                                ALU.subtract).then_inc(lo_a_ready, 1)

            lo_a(0, 0, True)
            lo_a(1, 1, False)
            with pool.Fori(1, PAIRS // TRING) as it:
                for s in range(TRING):
                    lo_a(it * TRING + s, s, False)

        PIECES = H // PIECE
        assert PIECES == NF and all(b % PIECE == 0 for _, b in REST)

        def pieces_done(pair, c, first):
            return c + 1 if first else pair * PIECES + REST[c][1] // PIECE

        @block.scalar
        def _(act):
            act.dma_start(w_raw[:], w.rearrange("o c h w -> o (c h w)")).then_inc(w_loaded, 16)

            def deviation(pair, s):
                act.wait_ge(var_ready, pair + 1)
                nc.scalar.activation(std[:], var[:], ACT.Sqrt,
                                     bias=zero[:]).then_inc(std_ready, 1)

            def normalise(pair, s, slot, a, b):
                nc.scalar.activation(xnorm[:, slot, a * W:b * W], xbuf[:, s, a * W:b * W], ACT.Identity,
                                     bias=coef[:, s, 1:2], scale=coef[:, s, 0:1]).then_inc(xnorm_ready, 1)

            def hi(slot, a, b):
                nc.scalar.copy(inner(1, slot, ALL, a, b),
                               rows(xnorm[:, slot, :], a, b)).then_inc(hi_ready, 1)

            def hi_a(slot, a, b):
                nc.scalar.copy(inner(0, slot, HIGH, a, b),
                               rows(xnorm[LOW, slot, :], a, b)).then_inc(hi_a_ready, 1)

            act.wait_ge(zero_ready, 1)
            nc.scalar.activation(warm[:], zero[:], ACT.Sqrt, bias=zero[:])
            act.wait_ge(w_turned, 1)
            nc.scalar.copy(w_taps[:, 0:8, :], psum[:, 0, :].rearrange("p (t o) -> p t o", o=CO)).then_inc(w_ready, 1)
            nc.scalar.copy(w_taps[:, 8, :], psum[:, 1, 0:CO]).then_inc(w_ready, 1)
            deviation(0, 0)
            act.wait_ge(coef_ready, 2)
            for c, (a, b) in enumerate(FIRST):
                normalise(0, 0, 0, a, b)
                act.wait_ge(xnorm_ready, c + 1)
                hi(0, a, b)
                hi_a(0, a, b)

            def pair_after(pair, s, slot, free):
                deviation(pair, s)
                act.wait_ge(coef_ready, 2 * (pair + 1))
                if free:
                    act.wait_ge(lo_b_ready, chunks_done(pair - NRING, NR - 1))
                for a, b in REST:
                    normalise(pair, s, slot, a, b)
                if free:
                    act.wait_ge(conv_done, (pair - TRING + 1) * NB)
                for c, (a, b) in enumerate(REST):
                    act.wait_ge(xnorm_ready, chunks_done(pair, c))
                    hi(slot, a, b)
                    hi_a(slot, a, b)

            deviation(1, 1)
            act.wait_ge(coef_ready, 4)
            for c, (a, b) in enumerate(REST):
                normalise(1, 1, 1, a, b)
                act.wait_ge(xnorm_ready, chunks_done(1, c))
                hi(1, a, b)
                hi_a(1, a, b)
            act.wait_ge(lo_b_ready, NF)
            pair_after(2, 2, 0, True)
            pair_after(3, 3, 1, True)
            with act.Fori(1, PAIRS // XRING) as it:
                for s in range(XRING):
                    pair_after(it * XRING + s, s, s % TRING, True)

        @block.vector
        def _(dve):
            nc.vector.memset(zero[:], 0.0).then_inc(zero_ready, 1)

            dve.wait_ge(w_loaded, 16)
            nc.vector.tensor_scalar(w_pos[:], w_raw[:], 0.0, -1.0, ALU.is_gt, ALU.add).then_inc(w_step, 1)
            dve.wait_ge(w_step, 1)
            nc.vector.scalar_tensor_tensor(w_sign[:], w_raw[:].rearrange("o (c t) -> o t c", t=TAPS), 0.0,
                                           w_pos[:].rearrange("o (c t) -> o t c", t=TAPS),
                                           ALU.is_ge, ALU.add).then_inc(w_step, 1)

            def block_stats(s, blocks):
                for n in blocks:
                    nc.vector.bn_stats(stats[:, s % 2, n, :], xbuf[:, s, n * BN:(n + 1) * BN]).then_inc(blocks_ready, 1)

            STEPS = 10

            def wait_blocks(pair):
                dve.wait_ge(blocks_ready, (pair + 1) * NB)

            def aggregate(s):
                nc.vector.bn_aggr(own[:], stats[:, s % 2]).then_inc(coef_step, 1)

            def swap(pair):
                dve.wait_ge(coef_step, pair * STEPS + 1)
                nc.vector.tensor_scalar(half_mean[:], own[:, 0:1], -0.5, None, ALU.mult).then_inc(coef_step, 1)
                nc.vector.stream_shuffle(other[:], own[:], [i ^ 1 for i in range(32)]).then_inc(coef_step, 1)

            def combine(pair):
                dve.wait_ge(coef_step, pair * STEPS + 3)
                nc.vector.tensor_scalar(apart[:], own[:, 0:1], other[:, 0:1], 0.5 / SCALE,
                                        ALU.subtract, ALU.mult).then_inc(coef_step, 1)
                nc.vector.tensor_scalar(within[:], own[:, 1:2], other[:, 1:2], 0.5 / SCALE ** 2,
                                        ALU.add, ALU.mult).then_inc(coef_step, 1)
                nc.vector.tensor_scalar(neg_mean[:], other[:, 0:1], -0.5, half_mean[:],
                                        ALU.mult, ALU.add).then_inc(coef_step, 1)

            def between(pair):
                dve.wait_ge(coef_step, pair * STEPS + 6)
                nc.vector.tensor_scalar(square[:], apart[:], apart[:], EPS / SCALE ** 2,
                                        ALU.mult, ALU.add).then_inc(coef_step, 1)

            def variance(pair):
                dve.wait_ge(coef_step, pair * STEPS + 7)
                nc.vector.tensor_tensor(var[:], within[:], square[:], ALU.add).then_inc(var_ready, 1)

            def inverse(pair):
                dve.wait_ge(std_ready, pair + 1)
                nc.vector.reciprocal(inv[:], std[:]).then_inc(coef_step, 1)

            def newton_a(pair):
                dve.wait_ge(coef_step, pair * STEPS + 8)
                nc.vector.tensor_scalar(ratio[:], var[:], inv[:], inv[:], ALU.mult, ALU.mult).then_inc(coef_step, 1)

            def newton_b(pair):
                dve.wait_ge(coef_step, pair * STEPS + 9)
                nc.vector.tensor_scalar(factor[:], ratio[:], -0.5, 1.5, ALU.mult, ALU.add).then_inc(coef_step, 1)

            def scale_and_bias(pair, s):
                dve.wait_ge(coef_step, pair * STEPS + 10)
                nc.vector.tensor_scalar(coef[:, s, 0:1], factor[:], inv[:], None, ALU.mult).then_inc(coef_ready, 1)
                nc.vector.tensor_scalar(coef[:, s, 1:2], factor[:], inv[:], neg_mean[:],
                                        ALU.mult, ALU.mult).then_inc(coef_ready, 1)

            def lo_b(pair, slot, c, first=False):
                a, b = chunks(first)[c]
                dve.wait_ge(hi_ready, c + 1 if first else chunks_done(pair, c))
                dve.wait_ge(lo_a_ready, pieces_done(pair, c, first))
                nc.vector.tensor_tensor(inner(1, slot, LOW, a, b), rows(xnorm[HIGH, slot, :], a, b),
                                        inner(1, slot, HIGH, a, b), ALU.subtract).then_inc(lo_b_ready, 1)

            def evacuate(pair, s, g):
                b0, n = GR[g][0], len(GR[g])
                dve.wait_ge(conv_done, pair * NB + b0 + n)
                x_part = xbuf[:, s, b0 * BN:(b0 + n) * BN].rearrange("p (n m) -> p n m", m=BN)
                out_part = obuf[:, s % ORING, b0 * BN:(b0 + n) * BN].rearrange("p (n m) -> p n m", m=BN)
                nc.vector.scalar_tensor_tensor(out_part, psum[:, b0:b0 + n, 0:BN], 1.0 / SCALE, x_part,
                                               ALU.mult, ALU.add).then_inc(evacuated, 1)

            for g, blocks in enumerate(GR):
                dve.wait_ge(x0_loaded[g], 16)
                block_stats(0, blocks)
            wait_blocks(0)
            aggregate(0)
            swap(0)
            combine(0)
            between(0)
            variance(0)
            inverse(0)
            newton_a(0)
            newton_b(0)
            scale_and_bias(0, 0)

            def part_loaded(it, s, h):
                dve.wait_ge(loaded[s][h], loads_done(it, s))

            def stats_of(it, s, blocks):
                for n in blocks:
                    for h, groups in enumerate(PARTS):
                        if n == GR[groups[0]][0]:
                            part_loaded(it, s, h)
                    block_stats(s, [n])

            stats_of(0, 1, range(0, 3))
            lo_b(0, 0, 0, True)
            stats_of(0, 1, range(3, NB))
            wait_blocks(1)
            aggregate(1)
            swap(1)
            combine(1)
            between(1)
            variance(1)
            lo_b(0, 0, 1, True)
            inverse(1)
            stats_of(0, 2, range(0, 1))
            newton_a(1)
            lo_b(0, 0, 2, True)
            newton_b(1)
            stats_of(0, 2, range(1, 2))
            scale_and_bias(1, 1)
            stats_of(0, 2, range(2, 5))
            lo_b(0, 0, 3, True)
            stats_of(0, 2, range(5, NB))
            wait_blocks(2)

            def pair_step(it, s, lo, coefs, blocks):
                pair = it * XRING + s
                slot1, slot2, slot3 = (s + 1) % TRING, (s + 2) % XRING, (s + 3) % XRING
                turn3 = it + (s + 3) // XRING

                def after_next(step, *args):
                    if coefs:
                        step(*args)

                def third(n):
                    if blocks:
                        stats_of(turn3, slot3, [n])

                if not blocks:
                    for h in range(NP):
                        dve.wait_ge(stored[s % ORING][h], 16 * (stores_done(it, s) - 1))
                after_next(aggregate, slot2)
                third(0)
                after_next(swap, pair + 2)
                third(1)
                after_next(combine, pair + 2)
                evacuate(pair, s, 0)
                after_next(between, pair + 2)
                third(2)
                after_next(variance, pair + 2)
                if lo:
                    lo_b(pair + 1, slot1, 0)
                after_next(inverse, pair + 2)
                evacuate(pair, s, 1)
                after_next(newton_a, pair + 2)
                third(3)
                after_next(newton_b, pair + 2)
                third(4)
                after_next(scale_and_bias, pair + 2, slot2)
                if lo:
                    lo_b(pair + 1, slot1, 1)
                evacuate(pair, s, 2)
                third(5)
                third(6)
                if blocks:
                    wait_blocks(pair + 3)
                evacuate(pair, s, 3)

            with dve.Fori(0, PAIRS // XRING - 1) as it:
                for s in range(XRING):
                    pair_step(it, s, True, True, True)
            for s in range(XRING):
                pair_step(PAIRS // XRING - 1, s, s + 1 < XRING, s + 2 < XRING, s + 3 < XRING)

        @block.tensor
        def _(pe):
            pe.wait_ge(ident_step, 2)
            pe.wait_ge(w_step, 2)
            for t in range(TAPS):
                for lanes in (LOW, HIGH):
                    mm = pe.matmul(psum[lanes, t // 8, (t % 8) * CO:(t % 8 + 1) * CO],
                                   w_sign[:, t, :], ident[:], start=True, stop=True)
            mm.then_inc(w_turned, 1)
            for _ in range(WARM_UP):
                pe.matmul(psum[LOW, 7, :], w_sign[:, 0, :], w_sign[:].rearrange("o t c -> o (t c)")[:, 0:512],
                          start=True, stop=True)

            ORDER = sorted(range(TAPS), key=lambda t: abs(t // KW - 1))

            def convolve(pair, slot, first=False, banks_used=True):
                for n in range(NB):
                    last_row = min((n + 1) * BR, H - 1)
                    c = chunk_of_row(last_row, first)
                    if n == 0 or c != chunk_of_row(min(n * BR, H - 1), first):
                        done = c + 1 if first else chunks_done(pair, c)
                        pe.wait_ge(hi_a_ready, done)
                        pe.wait_ge(lo_a_ready, pieces_done(pair, c, first))
                        pe.wait_ge(lo_b_ready, done)
                    if banks_used and n in [g[0] for g in GR]:
                        g = [g[0] for g in GR].index(n)
                        pe.wait_ge(evacuated, (pair - 1) * NG + g + 1)
                    for k, t in enumerate(ORDER):
                        dy, dx = t // KW - 1, t % KW - 1
                        a, b = max(n * BR, -dy), min((n + 1) * BR, H - dy)
                        for img, cols in enumerate((LOW, HIGH)):
                            at = (a + dy) * PW + LEAD + dx
                            v = halves[:, slot, img, at:at + (b - a) * PW].rearrange("p (h w) -> p h w", w=PW)
                            mm = pe.matmul(psum[cols, n, (a - n * BR) * W:(b - n * BR) * W], w_taps[:, t, :],
                                           v[:, :, 0:W],
                                           start=(k == 0), stop=(k == TAPS - 1))
                    mm.then_inc(conv_done, 1)

            pe.wait_ge(w_ready, 2)
            pe.wait_ge(borders_ready, 1)
            convolve(0, 0, first=True, banks_used=False)
            convolve(1, 1)
            with pe.Fori(1, PAIRS // TRING) as it:
                for s in range(TRING):
                    convolve(it * TRING + s, s)


_INS = ["x", "L0_conv_W"]


def kernel(**inputs):
    import numpy as _np
    import concourse.bacc as _bacc
    from concourse import mybir as _mybir
    from concourse.bass_utils import run_bass_kernel_spmd as _run

    nc = _bacc.Bacc("TRN2", target_bir_lowering=False, num_devices=1)
    arrays, args = {}, []
    for name in _INS:
        a = _np.ascontiguousarray(inputs[name])
        arrays[f"in_{name}_dram"] = a
        args.append(nc.dram_tensor(f"in_{name}_dram", a.shape, _mybir.dt.from_np(a.dtype), kind="ExternalInput").ap())
    shape = tuple(inputs["x"].shape)
    args.append(nc.dram_tensor("out_0_dram", shape, _mybir.dt.float32, kind="ExternalOutput").ap())
    conv_preact_kernel(nc, *args)
    r = _run(nc, [arrays], core_ids=[0])
    return r.results[0]["out_0_dram"]
```

```python
from contextlib import ExitStack

import concourse.bass as bass
from concourse import mybir


F32 = mybir.dt.float32
F16 = mybir.dt.float16
ALU = mybir.AluOpType
ACT = mybir.ActivationFunctionType

GROUPS = 32
EPS = 1e-5
SCALE = 2.0 ** 9

XRING = 4
ORING = 4
TRING = 2
NRING = 2
WARM_UP = 26


def conv_preact_kernel(nc: bass.Bass, x: bass.AP, w: bass.AP, out: bass.AP):
    B, C, H, W = x.shape
    CO, _, KH, KW = w.shape
    assert 2 * C == 128 and CO == C and C // GROUPS == 2 and KH == KW == 3
    assert (C // GROUPS) * H * W * SCALE ** 2 < 65504.0 ** 2
    PAIRS = B // 2
    HW = H * W
    BR = 8
    BN = BR * W
    NB = H // BR
    TAPS = KH * KW
    GR = [range(0, 2), range(2, 4), range(4, 6), range(6, 7)]
    NG = len(GR)
    PARTS = [range(0, 2), range(2, NG)]
    NP = len(PARTS)
    LOADS0 = [range(0, 2), range(2, 4), range(4, 5), range(5, 6), range(6, 7)]

    def elements(blocks):
        return slice(blocks[0] * BN, (blocks[-1] + 1) * BN)

    def part_of(groups):
        return slice(GR[groups[0]][0] * BN, (GR[groups[-1]][-1] + 1) * BN)

    assert BN <= 512 and H % BR == 0 and GR[-1][-1] == LOADS0[-1][-1] == NB - 1
    assert PAIRS % XRING == 0 and PAIRS > XRING and XRING % TRING == 0 and TRING == NRING
    assert ORING == XRING

    FIRST = [(0, 9), (9, 17), (17, 25), (25, 41), (41, 56)]
    REST = [(0, 14), (14, 28), (28, 42), (42, 56)]
    NF, NR = len(FIRST), len(REST)
    POOL_B = [3, 2]
    EARLY = [NF - 1, 2]

    def chunks(first):
        return FIRST if first else REST

    def chunks_done(pair, c, first):
        return c + 1 if first else (pair - 1) * NR + NF + c + 1

    def chunk_of_row(row, first):
        return next(c for c, (a, b) in enumerate(chunks(first)) if a <= row < b)

    x_pairs = x.rearrange("(n b) c h w -> n (b c) (h w)", b=2)
    out_pairs = out.rearrange("(n b) c h w -> n (b c) (h w)", b=2)

    with ExitStack() as ctx:
        def sb(name, shape, dt):
            return ctx.enter_context(nc.sbuf_tensor(name, shape, dt))

        def sem(name):
            return ctx.enter_context(nc.semaphore(name))

        xbuf = sb("xbuf", [128, XRING, HW], F32)
        obuf = sb("obuf", [128, ORING, HW], F32)
        xnorm = sb("xnorm", [128, NRING, HW], F32)
        halves = sb("halves", [128, TRING, 2, HW], F16)
        w_raw = sb("w_raw", [CO, C * TAPS], F32)
        w_pos = sb("w_pos", [CO, C * TAPS], F32)
        w_sign = sb("w_sign", [CO, TAPS, C], F16)
        w_taps = sb("w_taps", [128, TAPS, CO], F16)
        ident = sb("ident", [CO, CO], F16)
        stats = sb("stats", [128, 2, NB, 6], F32)
        own = sb("own", [128, 2], F32)
        other = sb("other", [128, 2], F32)
        half_mean, neg_mean, half_var, apart, within, var, std, inv, dev = [
            sb(name, [128, 1], F32) for name in
            ("half_mean", "neg_mean", "half_var", "apart", "within", "var", "std", "inv", "dev")]
        coef = sb("coef", [128, XRING, 2], F32)
        zero = sb("zero", [128, 1], F32)
        warm = sb("warm", [128, 1], F32)
        psum = ctx.enter_context(nc.psum_tensor("psum", [128, 8, 512], F32))

        x0_loaded = [sem(f"x0_loaded{h}") for h in range(len(LOADS0))]
        loaded = [[sem(f"loaded{s}_{h}") for h in range(NP)] for s in range(XRING)]
        stored = [[sem(f"stored{s}_{h}") for h in range(NP)] for s in range(ORING)]
        last_stored = sem("last_stored")
        w_loaded = sem("w_loaded")
        w_step = sem("w_step")
        ident_step = sem("ident_step")
        zero_ready = sem("zero_ready")
        w_turned = sem("w_turned")
        w_ready = sem("w_ready")
        blocks_ready = sem("blocks_ready")
        coef_step = sem("coef_step")
        var_ready = sem("var_ready")
        std_ready = sem("std_ready")
        coef_ready = sem("coef_ready")
        xnorm_early = sem("xnorm_early")
        xnorm_ready = sem("xnorm_ready")
        hi_ready = sem("hi_ready")
        hi_a_ready = sem("hi_a_ready")
        lo_a_first = sem("lo_a_first")
        lo_a_ready = sem("lo_a_ready")
        lo_b_ready = sem("lo_b_ready")
        conv_done = sem("conv_done")
        evacuated = sem("evacuated")

        def rows(t, a, b):
            return t[:, a * W:b * W].rearrange("p (h w) -> p h w", w=W)

        def half_rows(img, slot, lanes, a, b):
            return rows(halves[lanes, slot, img, :], a, b)

        LOW, HIGH, ALL = slice(0, 64), slice(64, 128), slice(0, 128)

        def loads_done(it, s):
            return 16 * (it + 1) if s else 16 * it

        def early_done(pair, c):
            return sum(EARLY[:pair]) + c + 1

        block = ctx.enter_context(nc.Block())

        @block.sync
        def _(sp):
            sp.dma_start(w_raw[:], w.rearrange("o c h w -> o (c h w)")).then_inc(w_loaded, 16)
            for h, blocks in enumerate(LOADS0):
                part = elements(blocks)
                sp.dma_start(xbuf[:, 0, part], x_pairs[0][:, part]).then_inc(x0_loaded[h], 16)
            for s in range(1, XRING):
                for h, groups in enumerate(PARTS):
                    part = part_of(groups)
                    sp.dma_start(xbuf[:, s, part], x_pairs[s][:, part]).then_inc(loaded[s][h], 16)

            def store(pair, s, groups, done):
                sp.wait_ge(evacuated, pair * NG + groups[-1] + 1)
                part = part_of(groups)
                sp.dma_start(out_pairs[pair][:, part], obuf[:, s, part]).then_inc(done, 16)

            def store_and_load(pair, it, s, first=False):
                if not (first and s < 2):
                    for h in range(NP):
                        sp.wait_ge(stored[(s - 2) % ORING][h], 16 * (it + 1) if s >= 2 else 16 * it)
                for h, groups in enumerate(PARTS):
                    part = part_of(groups)
                    sp.wait_ge(evacuated, pair * NG + groups[-1] + 1)
                    sp.dma_start(xbuf[:, s, part], x_pairs[pair + XRING][:, part]).then_inc(loaded[s][h], 16)
                    store(pair, s, groups, stored[s][h])

            for s in range(XRING):
                store_and_load(s, 0, s, first=True)
            with sp.Fori(1, PAIRS // XRING - 1) as it:
                for s in range(XRING):
                    store_and_load(it * XRING + s, it, s)
            for s in range(XRING):
                pair = PAIRS - XRING + s
                if s < XRING - 1:
                    for h, groups in enumerate(PARTS):
                        store(pair, s, groups, stored[s][h])
                else:
                    for g in range(NG):
                        store(pair, s, [g], last_stored)
            sp.wait_ge(last_stored, 16 * NG)
            for s in range(XRING):
                for h in range(NP):
                    pairs_stored = PAIRS // XRING - (s == XRING - 1)
                    sp.wait_ge(stored[s][h], 16 * pairs_stored)

        def lo_a_done(pair, c, first):
            return chunks_done(pair, c, first) - 1

        @block.gpsimd
        def _(pool):
            nc.gpsimd.memset(ident[:], 0.0).then_inc(ident_step, 1)
            pool.wait_ge(ident_step, 1)
            nc.gpsimd.affine_select(out=ident[:], in_=ident[:], compare_op=ALU.not_equal, fill=1.0,
                                    base=0, pattern=[[-1, CO]], channel_multiplier=1).then_inc(ident_step, 1)

            def lo_a(pair, slot, c, first=False, early=False):
                a, b = chunks(first)[c]
                if early and c < EARLY[pair]:
                    pool.wait_ge(xnorm_early, early_done(pair, c))
                pool.wait_ge(hi_ready, chunks_done(pair, c, first))
                nc.gpsimd.tensor_tensor(half_rows(0, slot, LOW, a, b), rows(xnorm[LOW, slot, :], a, b),
                                        half_rows(1, slot, LOW, a, b), ALU.subtract).then_inc(lo_a_ready, 1)

            def lo_b(pair, slot, c, first=False):
                a, b = chunks(first)[c]
                pool.wait_ge(lo_a_ready, lo_a_done(pair, c, first))
                pool.wait_ge(lo_b_ready, chunks_done(pair, c - 1, first))
                nc.gpsimd.tensor_tensor(half_rows(1, slot, LOW, a, b), rows(xnorm[HIGH, slot, :], a, b),
                                        half_rows(1, slot, HIGH, a, b), ALU.subtract).then_inc(lo_b_ready, 1)

            for c in range(1, NF):
                lo_a(0, 0, c, first=True, early=True)
                if c >= POOL_B[0]:
                    lo_b(0, 0, c, first=True)
            for c in range(NR):
                lo_a(1, 1, c, early=True)
                if c >= POOL_B[1]:
                    lo_b(1, 1, c)
            with pool.Fori(1, PAIRS // TRING) as it:
                for s in range(TRING):
                    for c in range(NR):
                        lo_a(it * TRING + s, s, c)

        @block.scalar
        def _(act):
            def deviation(pair):
                act.wait_ge(var_ready, pair + 1)
                nc.scalar.activation(std[:], var[:], ACT.Sqrt,
                                     bias=zero[:]).then_inc(std_ready, 1)

            def normalise(s, slot, a, b):
                nc.scalar.activation(xnorm[:, slot, a * W:b * W], xbuf[:, s, a * W:b * W], ACT.Identity,
                                     bias=coef[:, s, 1:2], scale=coef[:, s, 0:1]).then_inc(xnorm_ready, 1)

            def hi(slot, a, b):
                nc.scalar.copy(half_rows(1, slot, ALL, a, b),
                               rows(xnorm[:, slot, :], a, b)).then_inc(hi_ready, 1)

            def hi_a(slot, a, b):
                nc.scalar.copy(half_rows(0, slot, HIGH, a, b),
                               rows(xnorm[LOW, slot, :], a, b)).then_inc(hi_a_ready, 1)

            def hi_from_x(s, a, b):
                nc.scalar.activation(half_rows(1, s, ALL, a, b), rows(xbuf[:, s, :], a, b), ACT.Identity,
                                     bias=coef[:, s, 1:2], scale=coef[:, s, 0:1]).then_inc(hi_ready, 1)

            def hi_a_from_x(s, a, b):
                nc.scalar.activation(half_rows(0, s, HIGH, a, b), rows(xbuf[LOW, s, :], a, b), ACT.Identity,
                                     bias=coef[LOW, s, 1:2], scale=coef[LOW, s, 0:1]).then_inc(hi_a_ready, 1)

            def own_chunks_done(pair, c, first=False):
                return chunks_done(pair, c, first) - (EARLY[0] if first else sum(EARLY))

            act.wait_ge(zero_ready, 1)
            nc.scalar.activation(warm[:], zero[:], ACT.Sqrt, bias=zero[:])
            act.wait_ge(w_turned, 1)
            nc.scalar.copy(w_taps[:, 0:8, :], psum[:, 0, :].rearrange("p (t o) -> p t o", o=CO)).then_inc(w_ready, 1)
            nc.scalar.copy(w_taps[:, 8, :], psum[:, 1, 0:CO]).then_inc(w_ready, 1)
            deviation(0)
            act.wait_ge(coef_ready, 2)
            for c in range(EARLY[0]):
                hi_from_x(0, *FIRST[c])
                if c > 0:
                    hi_a_from_x(0, *FIRST[c - 1])
            normalise(0, 0, *FIRST[NF - 1])
            hi_a_from_x(0, *FIRST[NF - 2])
            act.wait_ge(xnorm_ready, own_chunks_done(0, NF - 1, first=True))
            hi(0, *FIRST[NF - 1])
            hi_a(0, *FIRST[NF - 1])

            deviation(1)
            act.wait_ge(coef_ready, 2 * 2)
            hi_from_x(1, *REST[0])
            normalise(1, 1, *REST[2])
            hi_from_x(1, *REST[1])
            hi_a_from_x(1, *REST[0])
            act.wait_ge(xnorm_ready, own_chunks_done(1, 2))
            hi(1, *REST[2])
            hi_a_from_x(1, *REST[1])
            normalise(1, 1, *REST[3])
            hi_a(1, *REST[2])
            act.wait_ge(xnorm_ready, own_chunks_done(1, 3))
            hi(1, *REST[3])
            hi_a(1, *REST[3])

            def pair_after(pair, s, slot, back):
                deviation(pair)
                act.wait_ge(coef_ready, 2 * (pair + 1))
                act.wait_ge(lo_b_ready, back)
                normalise(s, slot, *REST[0])
                normalise(s, slot, *REST[1])
                act.wait_ge(conv_done, (pair - TRING + 1) * NB)
                for c in range(NR):
                    act.wait_ge(xnorm_ready, own_chunks_done(pair, c))
                    hi(slot, *REST[c])
                    if c > 0:
                        hi_a(slot, *REST[c - 1])
                    if c + 2 < NR:
                        normalise(s, slot, *REST[c + 2])
                hi_a(slot, *REST[NR - 1])

            pair_after(2, 2, 0, NF)
            pair_after(3, 3, 1, chunks_done(1, NR - 1, False))
            with act.Fori(1, PAIRS // XRING) as it:
                for s in range(XRING):
                    pair = it * XRING + s
                    pair_after(pair, s, s % TRING, chunks_done(pair - NRING, NR - 1, False))

        @block.vector
        def _(dve):
            nc.vector.memset(zero[:], 0.0).then_inc(zero_ready, 1)

            dve.wait_ge(w_loaded, 16)
            nc.vector.tensor_scalar(w_pos[:], w_raw[:], 0.0, -1.0, ALU.is_gt, ALU.add).then_inc(w_step, 1)
            dve.wait_ge(w_step, 1)
            nc.vector.scalar_tensor_tensor(w_sign[:], w_raw[:].rearrange("o (c t) -> o t c", t=TAPS), 0.0,
                                           w_pos[:].rearrange("o (c t) -> o t c", t=TAPS),
                                           ALU.is_ge, ALU.add).then_inc(w_step, 1)

            def block_stats(s, blocks):
                for n in blocks:
                    nc.vector.bn_stats(stats[:, s % 2, n, :], xbuf[:, s, n * BN:(n + 1) * BN]).then_inc(blocks_ready, 1)

            STEPS = 9
            QUARTER = 0.25 / SCALE ** 2

            def wait_blocks(pair):
                dve.wait_ge(blocks_ready, (pair + 1) * NB)

            def aggregate(s):
                nc.vector.bn_aggr(own[:], stats[:, s % 2]).then_inc(coef_step, 1)

            def swap(pair):
                dve.wait_ge(coef_step, pair * STEPS + 1)
                nc.vector.tensor_scalar(half_mean[:], own[:, 0:1], -0.5, None, ALU.mult).then_inc(coef_step, 1)
                nc.vector.stream_shuffle(other[:], own[:], [i ^ 1 for i in range(32)]).then_inc(coef_step, 1)
                nc.vector.tensor_scalar(half_var[:], own[:, 1:2], 0.5 * QUARTER, EPS * QUARTER,
                                        ALU.mult, ALU.add).then_inc(coef_step, 1)

            def combine(pair):
                dve.wait_ge(coef_step, pair * STEPS + 4)
                nc.vector.tensor_scalar(apart[:], own[:, 0:1], other[:, 0:1], 0.5 * QUARTER ** 0.5,
                                        ALU.subtract, ALU.mult).then_inc(coef_step, 1)
                nc.vector.tensor_scalar(within[:], other[:, 1:2], 0.5 * QUARTER, half_var[:],
                                        ALU.mult, ALU.add).then_inc(coef_step, 1)
                nc.vector.tensor_scalar(neg_mean[:], other[:, 0:1], -0.5, half_mean[:],
                                        ALU.mult, ALU.add).then_inc(coef_step, 1)

            def variance(pair):
                dve.wait_ge(coef_step, pair * STEPS + 7)
                nc.vector.tensor_scalar(var[:], apart[:], apart[:], within[:],
                                        ALU.mult, ALU.add).then_inc(var_ready, 1)

            def inverse(pair):
                dve.wait_ge(std_ready, pair + 1)
                nc.vector.reciprocal(inv[:], std[:]).then_inc(coef_step, 1)

            def newton(pair):
                dve.wait_ge(coef_step, pair * STEPS + 8)
                nc.vector.tensor_scalar(dev[:], var[:], inv[:], std[:], ALU.mult, ALU.add).then_inc(coef_step, 1)

            def scale(pair, s):
                dve.wait_ge(coef_step, pair * STEPS + 9)
                nc.vector.reciprocal(coef[:, s, 0:1], dev[:]).then_inc(coef_ready, 1)

            def bias(pair, s):
                dve.wait_ge(coef_ready, 2 * pair + 1)
                nc.vector.tensor_scalar(coef[:, s, 1:2], neg_mean[:], coef[:, s, 0:1], None,
                                        ALU.mult).then_inc(coef_ready, 1)

            def normalise(s, c):
                a, b = chunks(s == 0)[c]
                dve.wait_ge(coef_ready, 2 * (s + 1))
                nc.vector.tensor_scalar(xnorm[:, s, a * W:b * W], xbuf[:, s, a * W:b * W],
                                        coef[:, s, 0:1], coef[:, s, 1:2],
                                        ALU.mult, ALU.add).then_inc(xnorm_early, 1)

            def lo_a_of_first():
                a, b = FIRST[0]
                dve.wait_ge(xnorm_early, 1)
                dve.wait_ge(hi_ready, 1)
                nc.vector.tensor_tensor(half_rows(0, 0, LOW, a, b), rows(xnorm[LOW, 0, :], a, b),
                                        half_rows(1, 0, LOW, a, b), ALU.subtract).then_inc(lo_a_first, 1)

            def lo_b(pair, slot, c, first=False):
                a, b = chunks(first)[c]
                dve.wait_ge(hi_ready, chunks_done(pair, c, first))
                if first and c == 0:
                    dve.wait_ge(lo_a_first, 1)
                else:
                    dve.wait_ge(lo_a_ready, lo_a_done(pair, c, first))
                nc.vector.tensor_tensor(half_rows(1, slot, LOW, a, b), rows(xnorm[HIGH, slot, :], a, b),
                                        half_rows(1, slot, HIGH, a, b), ALU.subtract).then_inc(lo_b_ready, 1)

            def evacuate(pair, s, g):
                b0, n = GR[g][0], len(GR[g])
                dve.wait_ge(conv_done, pair * NB + b0 + n)
                x_part = xbuf[:, s, b0 * BN:(b0 + n) * BN].rearrange("p (n m) -> p n m", m=BN)
                out_part = obuf[:, s, b0 * BN:(b0 + n) * BN].rearrange("p (n m) -> p n m", m=BN)
                nc.vector.scalar_tensor_tensor(out_part, psum[:, b0:b0 + n, 0:BN], 1.0 / SCALE, x_part,
                                               ALU.mult, ALU.add).then_inc(evacuated, 1)

            def stats_of(it, s, blocks):
                for n in blocks:
                    for h, groups in enumerate(PARTS):
                        if n == GR[groups[0]][0]:
                            dve.wait_ge(loaded[s][h], loads_done(it, s))
                    block_stats(s, [n])

            for h, blocks in enumerate(LOADS0):
                dve.wait_ge(x0_loaded[h], 16)
                block_stats(0, blocks)
            wait_blocks(0)
            aggregate(0)
            swap(0)
            combine(0)
            variance(0)
            inverse(0)
            newton(0)
            scale(0, 0)
            bias(0, 0)
            normalise(0, 0)
            normalise(0, 1)
            lo_a_of_first()
            lo_b(0, 0, 0, first=True)
            normalise(0, 2)
            normalise(0, 3)
            lo_b(0, 0, 1, first=True)
            stats_of(0, 1, [0, 1])
            lo_b(0, 0, 2, first=True)
            stats_of(0, 1, [2, 3, 4, 5, 6])
            wait_blocks(1)
            aggregate(1)
            swap(1)
            combine(1)
            variance(1)
            stats_of(0, 2, [0])
            inverse(1)
            newton(1)
            stats_of(0, 2, [1])
            scale(1, 1)
            bias(1, 1)
            for c in range(EARLY[1]):
                normalise(1, c)
            stats_of(0, 2, [2])
            evacuate(0, 0, 0)
            stats_of(0, 2, [3])
            lo_b(1, 1, 0)
            stats_of(0, 2, [4])
            lo_b(1, 1, 1)
            stats_of(0, 2, [5, 6])
            wait_blocks(2)
            aggregate(2)
            evacuate(0, 0, 1)
            swap(2)
            combine(2)
            variance(2)
            stats_of(0, 3, [0])
            inverse(2)
            newton(2)
            scale(2, 2)
            bias(2, 2)
            evacuate(0, 0, 2)
            stats_of(0, 3, [1, 2])
            evacuate(0, 0, 3)
            stats_of(0, 3, [3, 4, 5, 6])

            def pair_step(it, s, lo, coefs, blocks):
                pair = it * XRING + s
                slot1, slot2, slot3 = (s + 1) % TRING, (s + 2) % XRING, (s + 3) % XRING
                turn3 = it + (s + 3) // XRING

                def next_lo(c):
                    if lo:
                        lo_b(pair + 1, slot1, c)

                def after_next(step, *args):
                    if coefs:
                        step(*args)

                def third(*some):
                    if blocks:
                        stats_of(turn3, slot3, some)

                if not blocks:
                    for h in range(NP):
                        dve.wait_ge(stored[s][h], 16 * it)
                after_next(wait_blocks, pair + 2)
                evacuate(pair, s, 0)
                after_next(aggregate, slot2)
                next_lo(0)
                after_next(swap, pair + 2)
                third(0)
                after_next(combine, pair + 2)
                next_lo(1)
                after_next(variance, pair + 2)
                third(1)
                evacuate(pair, s, 1)
                after_next(inverse, pair + 2)
                third(2)
                after_next(newton, pair + 2)
                next_lo(2)
                after_next(scale, pair + 2, slot2)
                next_lo(3)
                after_next(bias, pair + 2, slot2)
                evacuate(pair, s, 2)
                third(3)
                evacuate(pair, s, 3)
                third(4, 5, 6)

            with dve.Fori(0, PAIRS // XRING - 1) as it:
                for p in range(1, XRING + 1):
                    pair_step(it + p // XRING, p % XRING, True, True, True)
            for s in range(1, XRING):
                pair_step(PAIRS // XRING - 1, s, s + 1 < XRING, s + 2 < XRING, False)

        @block.tensor
        def _(pe):
            pe.wait_ge(ident_step, 2)
            pe.wait_ge(w_step, 2)
            for t in range(TAPS):
                for lanes in (LOW, HIGH):
                    mm = pe.matmul(psum[lanes, t // 8, (t % 8) * CO:(t % 8 + 1) * CO],
                                   w_sign[:, t, :], ident[:], start=True, stop=True)
            mm.then_inc(w_turned, 1)
            pe.wait_ge(w_ready, 2)
            for _ in range(WARM_UP):
                for cols in (LOW, HIGH):
                    pe.matmul(psum[cols, 7, 0:7 * CO], w_taps[:, 0, :],
                              w_taps[:, 0:7, :].rearrange("p t o -> p (t o)"), start=True, stop=True)

            ORDER = sorted(range(TAPS), key=lambda t: (abs(t // KW - 1), abs(t % KW - 1)))

            def convolve(pair, slot, first=False, banks_used=True):
                for n in range(NB):
                    last_row = min((n + 1) * BR, H - 1)
                    c = chunk_of_row(last_row, first)
                    if n == 0 or c != chunk_of_row(min(n * BR, H - 1), first):
                        pe.wait_ge(hi_a_ready, chunks_done(pair, c, first))
                        if first and c == 0:
                            pe.wait_ge(lo_a_first, 1)
                        else:
                            pe.wait_ge(lo_a_ready, lo_a_done(pair, c, first))
                        pe.wait_ge(lo_b_ready, chunks_done(pair, c, first))
                    if banks_used and n in [g[0] for g in GR]:
                        g = [g[0] for g in GR].index(n)
                        pe.wait_ge(evacuated, (pair - 1) * NG + g + 1)
                    for k, t in enumerate(ORDER):
                        dy, dx = t // KW - 1, t % KW - 1
                        a, b = max(n * BR, -dy), min((n + 1) * BR, H - dy)
                        left, right = max(0, -dx), min(W, W - dx)
                        for img, cols in enumerate((LOW, HIGH)):
                            outs = psum[cols, n, 0:BN].rearrange("p (h w) -> p h w", w=W)
                            mm = pe.matmul(outs[:, a - n * BR:b - n * BR, left:right], w_taps[:, t, :],
                                           half_rows(img, slot, ALL, a + dy, b + dy)[:, :, left + dx:right + dx],
                                           start=(k == 0), stop=(k == TAPS - 1))
                    mm.then_inc(conv_done, 1)

            convolve(0, 0, first=True, banks_used=False)
            convolve(1, 1)
            with pe.Fori(1, PAIRS // TRING) as it:
                for s in range(TRING):
                    convolve(it * TRING + s, s)


_INS = ["x", "L0_conv_W"]


def kernel(**inputs):
    import numpy as _np
    import concourse.bacc as _bacc
    from concourse import mybir as _mybir
    from concourse.bass_utils import run_bass_kernel_spmd as _run

    nc = _bacc.Bacc("TRN2", target_bir_lowering=False, num_devices=1)
    arrays, args = {}, []
    for name in _INS:
        a = _np.ascontiguousarray(inputs[name])
        arrays[f"in_{name}_dram"] = a
        args.append(nc.dram_tensor(f"in_{name}_dram", a.shape, _mybir.dt.from_np(a.dtype), kind="ExternalInput").ap())
    shape = tuple(inputs["x"].shape)
    args.append(nc.dram_tensor("out_0_dram", shape, _mybir.dt.float32, kind="ExternalOutput").ap())
    conv_preact_kernel(nc, *args)
    r = _run(nc, [arrays], core_ids=[0])
    return r.results[0]["out_0_dram"]
```
